# Optimizing a Trainium2 kernel written in Bass

```python
import numpy as np
import jax
import jax.numpy as jnp

def _softmax(x, axis=-1):
    return jax.nn.softmax(x, axis=axis)

def _gelu(x):
    return jax.nn.gelu(x, approximate=True)

def _silu(x):
    return jax.nn.silu(x)

def _sigmoid(x):
    return jax.nn.sigmoid(x)

def _layernorm(x, axis=-1, eps=1e-05):
    m = jnp.mean(x, axis=axis, keepdims=True)
    v = jnp.var(x, axis=axis, keepdims=True)
    return (x - m) / jnp.sqrt(v + eps)

def _scatter_add(tgt, idx, src, axis=0):
    return tgt.at[idx].add(src)

def _segment_sum(src, seg, n):
    return jax.ops.segment_sum(src, seg, n)
kernel_name = 'mk_gnn_resnorm_d4_gnn_r8_74e9ff'

def setup_inputs(seed: int=0):
    np.random.seed(seed)
    _w = jnp.asarray

    def _rec_inputs():
        import jax
        import jax.numpy as jnp
        _gk = jax.random.key(seed)
        x = -0.000202 + 1 * jax.random.normal(jax.random.fold_in(_gk, 1), (12500, 64), jnp.float32)
        _s = jax.random.randint(jax.random.fold_in(_gk, 2), (200000,), 0, 12500, jnp.int32)
        _d = jax.random.randint(jax.random.fold_in(_gk, 3), (200000,), 0, 12500, jnp.int32)
        _loop = jnp.arange(12500, dtype=jnp.int32)
        src = jnp.concatenate([_s, _d, _loop])
        dst = jnp.concatenate([_d, _s, _loop])
        _o = jnp.argsort(dst, stable=True)
        src = src[_o]
        dst = dst[_o]
        edge_weight = jax.random.uniform(jax.random.fold_in(_gk, 13), (412500,), jnp.float32, 0.0, 0.999999)
        return (x, src, dst, edge_weight)
    x, src, dst, edge_weight = _rec_inputs()

    def _L0_gnn_setup():
        import jax, jax.numpy as jnp
        import numpy as np
        V = 12500
        E = 200000
        C_IN = 64
        C_OUT = 64
        key = jax.random.key(seed)
        k1, k2, k3, k4, k5 = jax.random.split(key, 5)
        features = jax.random.normal(k1, (V, C_IN), dtype=jnp.float32)
        src = jax.random.randint(k2, (E,), 0, V, dtype=jnp.int32)
        tgt = jnp.sort(jax.random.randint(k3, (E,), 0, V, dtype=jnp.int32))
        W = jax.random.normal(k4, (C_OUT, 2 * C_IN), dtype=jnp.float32) * (1.0 / np.sqrt(2 * C_IN))
        b = jax.random.normal(k5, (C_OUT,), dtype=jnp.float32) * 0.01
        return {'features': features, 'src': src, 'tgt': tgt, 'W': W, 'b': b}
    _L0_gnn_all = _L0_gnn_setup()
    _L0_gnn_in = {k: v for k, v in _L0_gnn_all.items() if k in ('W', 'b')}
    del _L0_gnn_all

    def _L1_gnn_setup():
        import jax, jax.numpy as jnp
        import numpy as np
        N_NODES = 12500
        N_EDGES = 200000
        C_IN = 64
        C_OUT = 64
        FILL = 2.0
        key = jax.random.key(seed)
        k1, k2, k3, k4 = jax.random.split(key, 4)
        x = jax.random.normal(k1, (N_NODES, C_IN), dtype=jnp.float32)
        edge_index = jax.random.randint(k2, (2, N_EDGES), 0, N_NODES, dtype=jnp.int64)
        edge_weight = jax.random.uniform(k3, (N_EDGES,), dtype=jnp.float32)
        W = jax.random.normal(k4, (C_IN, C_OUT), dtype=jnp.float32) / np.sqrt(C_IN)
        b = jnp.zeros((C_OUT,), dtype=jnp.float32)
        return {'x': x, 'edge_index': edge_index, 'edge_weight': edge_weight, 'W': W, 'b': b}
    _L1_gnn_all = _L1_gnn_setup()
    _L1_gnn_in = {k: v for k, v in _L1_gnn_all.items() if k in ('W', 'b')}
    del _L1_gnn_all

    def _L2_gnn_setup():
        import jax, jax.numpy as jnp
        import numpy as np
        N_NODES = 6250
        N_EDGES = 100000
        D_IN = 64
        D_OUT = 64
        key = jax.random.key(seed)
        k1, k2, k3, k4 = jax.random.split(key, 4)
        feat = jax.random.normal(k1, (N_NODES, D_IN), dtype=jnp.float32)
        limit = float(np.sqrt(6.0 / (D_IN + D_OUT)))
        weight = jax.random.uniform(k2, (D_IN, D_OUT), dtype=jnp.float32, minval=-limit, maxval=limit)
        bias = jnp.zeros((D_OUT,), dtype=jnp.float32)
        src = jax.random.randint(k3, (N_EDGES,), 0, N_NODES, dtype=jnp.int32)
        dst = jax.random.randint(k4, (N_EDGES,), 0, N_NODES, dtype=jnp.int32)
        return {'feat': feat, 'weight': weight, 'bias': bias, 'src': src, 'dst': dst}
    _L2_gnn_all = _L2_gnn_setup()
    _L2_gnn_in = {k: v for k, v in _L2_gnn_all.items() if k in ('weight', 'bias')}
    del _L2_gnn_all

    def _L3_gnn_setup():
        import jax, jax.numpy as jnp
        import numpy as np
        N_NODES = 12500
        N_EDGES = 125000
        DIM = 64
        key = jax.random.key(seed)
        k1, k2, k3, k4, k5, k6 = jax.random.split(key, 6)
        ego_embed = jax.random.normal(k1, (N_NODES, DIM), dtype=jnp.float32)
        edge_val = jax.random.uniform(k2, (N_EDGES,), dtype=jnp.float32)
        edge_src = jax.random.randint(k3, (N_EDGES,), 0, N_NODES, dtype=jnp.int32)
        edge_dst = jax.random.randint(k4, (N_EDGES,), 0, N_NODES, dtype=jnp.int32)
        lim = float(np.sqrt(6.0 / (DIM + DIM)))
        W_gc = jax.random.uniform(k5, (DIM, DIM), minval=-lim, maxval=lim, dtype=jnp.float32)
        W_bi = jax.random.uniform(k6, (DIM, DIM), minval=-lim, maxval=lim, dtype=jnp.float32)
        b_gc = jnp.zeros((DIM,), dtype=jnp.float32)
        b_bi = jnp.zeros((DIM,), dtype=jnp.float32)
        return {'ego_embed': ego_embed, 'edge_val': edge_val, 'W_gc': W_gc, 'b_gc': b_gc, 'W_bi': W_bi, 'b_bi': b_bi, 'edge_src': edge_src, 'edge_dst': edge_dst}
    _L3_gnn_all = _L3_gnn_setup()
    _L3_gnn_in = {k: v for k, v in _L3_gnn_all.items() if k in ('W_gc', 'b_gc', 'W_bi', 'b_bi')}
    del _L3_gnn_all
    return {'x': x, 'src': src, 'dst': dst, 'edge_weight': edge_weight, 'L0_gnn_W': _L0_gnn_in['W'], 'L0_gnn_b': _L0_gnn_in['b'], 'L1_gnn_W': _L1_gnn_in['W'], 'L1_gnn_b': _L1_gnn_in['b'], 'L2_gnn_weight': _L2_gnn_in['weight'], 'L2_gnn_bias': _L2_gnn_in['bias'], 'L3_gnn_W_gc': _L3_gnn_in['W_gc'], 'L3_gnn_b_gc': _L3_gnn_in['b_gc'], 'L3_gnn_W_bi': _L3_gnn_in['W_bi'], 'L3_gnn_b_bi': _L3_gnn_in['b_bi']}

def reference(x, src, dst, edge_weight, L0_gnn_W, L0_gnn_b, L1_gnn_W, L1_gnn_b, L2_gnn_weight, L2_gnn_bias, L3_gnn_W_gc, L3_gnn_b_gc, L3_gnn_W_bi, L3_gnn_b_bi):
    import jax
    import jax.numpy as jnp

    def _L0_gnn_ref(features, src, tgt, W, b):
        import jax, jax.numpy as jnp
        import numpy as np
        V = 12500
        E = 200000
        C_IN = 64
        C_OUT = 64
        num_v = features.shape[0]
        local = features[tgt]
        nbr = features[src]
        x = jnp.concatenate([local, nbr - local], axis=-1)
        y = jnp.einsum('ec,oc->eo', x, W) + b
        s = jax.ops.segment_sum(y, tgt, num_segments=num_v)
        cnt = jax.ops.segment_sum(jnp.ones((y.shape[0],), y.dtype), tgt, num_segments=num_v)
        cnt = cnt[:, None]
        return jnp.where(cnt > 0, s / jnp.maximum(cnt, 1.0), 0.0)

    def _L1_gnn_ref(x, edge_index, edge_weight, W, b):
        import jax, jax.numpy as jnp
        import numpy as np
        N_NODES = 12500
        N_EDGES = 200000
        C_IN = 64
        C_OUT = 64
        FILL = 2.0
        N = x.shape[0]
        src, dst = (edge_index[0], edge_index[1])
        loop = jnp.arange(N)
        src_f = jnp.concatenate([src, loop])
        dst_f = jnp.concatenate([dst, loop])
        w_f = jnp.concatenate([edge_weight, jnp.full((N,), FILL, dtype=x.dtype)])
        deg = jax.ops.segment_sum(w_f, dst_f, num_segments=N)
        dinv = jnp.where(deg > 0, jax.lax.rsqrt(deg), jnp.zeros_like(deg))
        norm = dinv[src_f] * w_f * dinv[dst_f]
        xw = x @ W
        msg = xw[src_f] * norm[:, None]
        out = jax.ops.segment_sum(msg, dst_f, num_segments=N) + b
        return jnp.tanh(out)

    def _L2_gnn_ref(feat, weight, bias, src, dst):
        import jax, jax.numpy as jnp
        import numpy as np
        N_NODES = 6250
        N_EDGES = 100000
        D_IN = 64
        D_OUT = 64
        n = feat.shape[0]
        deg = jax.ops.segment_sum(jnp.ones_like(dst, dtype=feat.dtype), dst, num_segments=n)
        norm = jnp.clip(deg, 1.0) ** (-0.5)
        h = feat * norm[:, None]
        agg = jax.ops.segment_sum(h[src], dst, num_segments=n)
        rst = agg @ weight
        rst = rst * norm[:, None] + bias
        return rst

    def _L3_gnn_ref(ego_embed, edge_val, W_gc, b_gc, W_bi, b_bi, edge_src, edge_dst):
        import jax, jax.numpy as jnp
        import numpy as np
        N_NODES = 12500
        N_EDGES = 125000
        DIM = 64
        n = ego_embed.shape[0]
        msgs = edge_val[:, None] * ego_embed[edge_src]
        neighbor_embed = jax.ops.segment_sum(msgs, edge_dst, num_segments=n)
        add_embed = jax.nn.leaky_relu((ego_embed + neighbor_embed) @ W_gc.T + b_gc)
        wise_embed = jax.nn.leaky_relu(ego_embed * neighbor_embed @ W_bi.T + b_bi)
        return add_embed + wise_embed
    edge_index = jnp.stack([src, dst])
    x = _layernorm(x + _L0_gnn_ref(x, src, dst, L0_gnn_W, L0_gnn_b), axis=-1)
    x = _layernorm(x + _L1_gnn_ref(x, edge_index, edge_weight, L1_gnn_W, L1_gnn_b), axis=-1)
    x = _layernorm(x + _L2_gnn_ref(x, L2_gnn_weight, L2_gnn_bias, src, dst), axis=-1)
    x = _layernorm(x + _L3_gnn_ref(x, edge_weight, L3_gnn_W_gc, L3_gnn_b_gc, L3_gnn_W_bi, L3_gnn_b_bi, src, dst), axis=-1)
    return x

_drawn_inputs = setup_inputs


def setup_inputs(seed=0):
    import zlib

    import numpy as np

    out = dict(_drawn_inputs(seed))
    spreads = {'L1_gnn_b': (0.0, 0.1),
     'L2_gnn_bias': (0.0, 0.1),
     'L3_gnn_b_gc': (0.0, 0.443),
     'L3_gnn_b_bi': (0.0, 0.45)}
    factors = {}
    for name, (base, spread) in spreads.items():
        noise = np.random.default_rng([zlib.crc32(name.encode()), seed]).standard_normal(out[name].shape)
        drawn = base * np.exp(spread * noise) if base else spread * noise
        out[name] = jnp.asarray(drawn.astype(out[name].dtype))
    for name, factor in factors.items():
        out[name] = (out[name] * factor).astype(out[name].dtype)
    return out
```

```python
import concourse.bass as bass
from concourse import mybir
from contextlib import ExitStack

F32 = mybir.dt.float32
I32 = mybir.dt.int32
U32 = mybir.dt.uint32
ALU = mybir.AluOpType
ACT = mybir.ActivationFunctionType
AX = mybir.AxisListType

P = 128
CHUNKS = 16
EDGE, GCN, NORM, BI = range(4)
WEIGHTED = (False, True, False, True)
EPS = 1e-5
SLOPE = 0.01
FILL = 2.0


def held(engine, value):
    return value if isinstance(value, int) else engine.to_reg(value)


class Chain:

    def __init__(self, engine, sem):
        self.engine, self.sem, self.base, self.k, self.turn, self.each = engine, sem, 0, 0, 0, 0

    def value(self):
        return self.base + self.turn * self.each + self.k if self.each else self.base + self.k

    def step(self, instruction):
        self.k += 1
        instruction.then_inc(self.sem, 1)
        self.engine.wait_ge(self.sem, self.value())

    def enter(self, turn, each):
        self.base, self.k, self.turn, self.each = self.base + self.k, 0, turn, each

    def leave(self, turns):
        assert self.k == self.each, (self.k, self.each)
        self.base, self.k, self.each = self.base + turns * self.each, 0, 0


def build(nc, x, src, dst, edge_weight, w0, b0, w1, b1, w2, b2, w_gc, b_gc, w_bi, b_bi, out):
    V, D = x.shape
    E = src.shape[0]
    GROUP = P * CHUNKS
    FULL = E // GROUP
    REST = E - FULL * GROUP
    TAIL_C = max(c for c in range(1, CHUNKS + 1) if REST % c == 0 and REST // c <= P)
    TAIL_P = REST // TAIL_C
    assert REST and TAIL_P <= P and FULL % 2 == 1
    NG = FULL + 1
    PAIRS = (FULL - 1) // 2
    TILES = -(-V // P)
    TB = 7
    NB = TILES // TB
    assert TILES == NB * TB and NB % 2 == 0
    VP = TILES * P
    BATCH = TB * P
    SR = D + 2

    tables = [x] + [nc.dram_tensor(f"table_{n}", (VP, D), F32, kind="Internal").ap() for n in (GCN, NORM, BI)]
    biases = (b0, b1, b2, b_gc, b_bi)

    with ExitStack() as ctx:
        def sb(name, shape, dt=F32):
            return ctx.enter_context(nc.sbuf_tensor(name, shape, dt))

        def ps(name, shape):
            return ctx.enter_context(nc.psum_tensor(name, shape, F32))

        def sem(name):
            return ctx.enter_context(nc.semaphore(name))

        src_ix = [sb(f"src_ix{s}", [P, CHUNKS], U32) for s in (0, 1)]
        dst_ix = [sb(f"dst_ix{s}", [P, CHUNKS], I32) for s in (0, 1)]
        weight = [sb(f"weight{s}", [P, CHUNKS]) for s in (0, 1)]
        first = [sb(f"first{s}", [P, 1], I32) for s in (0, 1)]
        offset = [sb(f"offset{s}", [P, CHUNKS]) for s in (0, 1)]
        match = [sb(f"match{s}", [P, CHUNKS, P]) for s in (0, 1)]
        rows = [sb(f"rows{s}", [P, CHUNKS, SR]) for s in (0, 1)]
        part = [ps(f"part{s}", [SR, P]) for s in (0, 1)]
        sums = sb("sums", [SR, VP + P])
        nodes = sb("nodes", [P, TILES, D])
        gcn_scale = sb("gcn_scale", [P, TILES])
        gcn_loop = sb("gcn_loop", [P, TILES])
        norm_scale = sb("norm_scale", [P, TILES])
        sums_b = [sb(f"sums_b{s}", [SR, BATCH]) for s in (0, 1)]
        nodes_b = [sb(f"nodes_b{s}", [P, TB, D]) for s in (0, 1)]
        feats_b = [sb(f"feats_b{s}", [D, BATCH]) for s in (0, 1)]
        prod_b = [sb(f"prod_b{s}", [D, BATCH]) for s in (0, 1)]
        result = [sb(f"result{s}", [P, TB, D]) for s in (0, 1)]
        work = sb("work", [P, TB, D])
        work2 = sb("work2", [P, TB, D])
        small = sb("small", [P, 8, 2 * TB])
        feats_ps = ps("feats_ps", [D, 1024])
        first_ps = ps("first_ps", [P, TB, SR])
        second_ps = ps("second_ps", [P, TB, D])
        ident = sb("ident", [P, P])
        iota_sb = sb("iota_sb", [P, P])
        iota = ps("iota", [P, P])
        ones = sb("ones", [P, 1])
        bias = sb("bias", [P, len(biases), D])
        w0_sb = sb("w0_sb", [D, 2, D])
        w0_own = sb("w0_own", [D, D])
        w0_sums = sb("w0_sums", [SR, SR])
        w1_sb = sb("w1_sb", [D, D])
        w2_sb = sb("w2_sb", [D, D])
        w_gc_sb = sb("w_gc_sb", [D, D])
        w_bi_sb = sb("w_bi_sb", [D, D])
        top = sb("top", [P, CHUNKS])
        low = sb("low", [P, CHUNKS])
        spread = sb("spread", [P, 4])
        flag = sb("flag", [1, 1], I32)
        outside = sb("outside", [P, CHUNKS, 2])

        s_loaded = [sem(f"s_loaded{s}") for s in (0, 1)]
        s_rows = [[sem(f"s_rows{n}_{s}") for s in (0, 1)] for n in range(4)]
        s_wcol = sem("s_wcol")
        s_offset = sem("s_offset")
        s_spread = sem("s_spread")
        s_equal = sem("s_equal")
        s_match = sem("s_match")
        s_part = sem("s_part")
        s_added = sem("s_added")
        s_cleared = sem("s_cleared")
        s_flag = sem("s_flag")
        s_out_ps = sem("s_out_ps")
        s_const = sem("s_const")
        s_nodes = sem("s_nodes")
        s_mem = sem("s_mem")
        s_ident = sem("s_ident")
        s_iota = sem("s_iota")
        s_prep = sem("s_prep")
        s_chain = sem("s_chain")
        s_staged = [sem(f"s_staged{n}") for n in range(4)]
        s_turned = [sem(f"s_turned{n}") for n in range(4)]
        s_feats = [sem(f"s_feats{n}") for n in range(4)]
        s_prods = [sem(f"s_prods{n}") for n in range(4)]
        s_taken = [sem(f"s_taken{n}") for n in range(4)]
        s_root_in = [sem(f"s_root_in{n}") for n in range(4)]
        s_root = [sem(f"s_root{n}") for n in range(4)]
        s_result = [sem(f"s_result{n}") for n in range(4)]
        s_stored = [[sem(f"s_stored{n}_{s}") for s in (0, 1)] for n in range(4)]
        r_loaded = [sem(f"r_loaded{n}") for n in range(4)]
        r_rows = [[sem(f"r_rows{n}_{j}") for j in (0, 1)] for n in range(4)]
        r_match = [sem(f"r_match{n}") for n in range(4)]
        r_part = [sem(f"r_part{n}") for n in range(4)]
        r_added = [sem(f"r_added{n}") for n in range(4)]

        block = ctx.enter_context(nc.Block())

        def shape_of(g):
            return (TAIL_P, TAIL_C) if isinstance(g, int) and g == FULL else (P, CHUNKS)

        def edges_of(array, g):
            p, c = shape_of(g)
            return array[bass.ds(g * GROUP, p * c)].rearrange("(p c) -> p c", c=c)

        def load_group(sp, g, s, loaded):
            p, c = shape_of(g)
            sp.dma_start(src_ix[s][0:p, 0:c].bitcast(I32), edges_of(src, g)).then_inc(loaded, 16)
            sp.dma_start(dst_ix[s][0:p, 0:c], edges_of(dst, g)).then_inc(loaded, 16)
            sp.dma_start(weight[s][0:p, 0:c], edges_of(edge_weight, g)).then_inc(loaded, 16)
            sp.dma_start(first[s][:, :], dst[bass.ds(g * GROUP, 1)].partition_broadcast(P)).then_inc(loaded, 16)

        LOADS = 4 * 16
        PER_SLOT = NG // 2

        ROOTS = (2, 2, 1, 1)
        SLOW = ((2, 5), (3, 4), (2, 4), (3, 4))

        @block.sync
        def _(sp):
            full_tiles = V // P
            with nc.allow_non_contiguous_dma(reason="weights are transposed and biases repeated once"):
                for n in range(4):
                    def load(g, s):
                        if not (isinstance(g, int) and n * NG + g < 2):
                            sp.wait_ge(s_added, n * NG - 1 + g)
                        load_group(sp, g, s, s_loaded[s])
                    load(0, 0)
                    load(1, 1)
                    if n == 0:
                        sp.dma_start(w0_sb[:, 0, :], w0[:, 0:D].rearrange("o c -> c o")).then_inc(s_const, 16)
                        sp.dma_start(w0_sb[:, 1, :], w0[:, D:2 * D].rearrange("o c -> c o")).then_inc(s_const, 16)
                        sp.dma_start(w1_sb[:, :], w1).then_inc(s_const, 16)
                        sp.dma_start(w2_sb[:, :], w2).then_inc(s_const, 16)
                        sp.dma_start(w_gc_sb[:, :], w_gc.rearrange("o c -> c o")).then_inc(s_const, 16)
                        sp.dma_start(w_bi_sb[:, :], w_bi.rearrange("o c -> c o")).then_inc(s_const, 16)
                        for k, b in enumerate(biases):
                            sp.dma_start(bias[:, k, :], b.partition_broadcast(P)).then_inc(s_const, 16)
                        sp.wait_ge(s_mem, 1)
                        sp.dma_start(nodes[:, 0:full_tiles, :],
                                     x[0:full_tiles * P, :].rearrange("(t p) f -> p t f", p=P)).then_inc(s_nodes, 16)
                        sp.dma_start(nodes[0:V - full_tiles * P, full_tiles, :],
                                     x[full_tiles * P:V, :]).then_inc(s_nodes, 16)
                    with sp.Fori(1, PAIRS) as i:
                        load(2 * i, 0)
                        load(2 * i + 1, 1)
                    load(FULL - 1, 0)
                    load(FULL, 1)

                    sp.wait_ge(s_flag, 1)
                    outside_any = sp.value_load(flag[0:1, 0:1], min_val=0, max_val=P)
                    with sp.If(outside_any > 0):
                        def reload(g, done):
                            sp.wait_ge(r_added[n], done)
                            load_group(sp, g, 0, r_loaded[n])
                        sp.wait_ge(s_added, (n + 1) * NG)
                        load_group(sp, 0, 0, r_loaded[n])
                        with sp.Fori(1, FULL) as g:
                            reload(g, g * TILES)
                        reload(FULL, FULL * TILES)

                    def store(b, s):
                        sp.wait_ge(s_result[n], b + 1)
                        sp.dma_start(tables[n + 1][bass.ds(b * BATCH, BATCH), :].rearrange("(t p) f -> p t f", p=P)
                                     if n < BI else
                                     out[bass.ds(b * BATCH, BATCH), :].rearrange("(t p) f -> p t f", p=P),
                                     result[s][:, :, :]).then_inc(s_stored[n][s], 16)
                    with sp.Fori(0, NB // 2 - 1) as i:
                        store(2 * i, 0)
                        store(2 * i + 1, 1)
                    store(NB - 2, 0)
                    if n < BI:
                        store(NB - 1, 1)
                    else:
                        at = (NB - 1) * BATCH
                        whole = (V - at) // P
                        sp.wait_ge(s_result[n], NB)
                        sp.dma_start(out[at:at + whole * P, :].rearrange("(t p) f -> p t f", p=P),
                                     result[1][:, 0:whole, :]).then_inc(s_stored[n][1], 16)
                        sp.dma_start(out[at + whole * P:V, :],
                                     result[1][0:V - at - whole * P, whole, :]).then_inc(s_stored[n][1], 16)
                sp.wait_ge(s_stored[BI][0], 16 * (NB // 2))
                sp.wait_ge(s_stored[BI][1], 16 * (NB // 2 + 1))

        @block.gpsimd
        def _(pool):
            nc.gpsimd.memset(ident[:, :], 0.0).then_inc(s_ident, 1)
            nc.gpsimd.iota(iota_sb[:, :], pattern=[[1, P]], base=0, channel_multiplier=0,
                           allow_small_or_imprecise_dtypes=True).then_inc(s_iota, 1)
            pool.wait_ge(s_ident, 1)
            nc.gpsimd.affine_select(out=ident[:, :], in_=ident[:, :], compare_op=ALU.not_equal, fill=1.0,
                                    base=0, pattern=[[-1, P]], channel_multiplier=1).then_inc(s_ident, 1)

            def gather(n, g, s, sems, single=False):
                p, c = shape_of(g)
                for j in range(c):
                    pool.indirect_dma_start(
                        rows[s][0:p, j, 0:D], None, tables[n][:, :],
                        bass.IndirectOffsetOnAxis(ap=src_ix[s][0:p, j:j + 1], axis=0),
                    ).then_inc(sems[j % len(sems)], 16)

            for n in range(4):
                def table_ready():
                    if n:
                        for s in (0, 1):
                            pool.wait_ge(s_stored[n - 1][s], 16 * (NB // 2))
                    else:
                        pool.wait_ge(s_ident, 2)

                def gather_group(g, s):
                    table_ready()
                    pool.wait_ge(s_loaded[s], LOADS * (n + 1) * PER_SLOT)
                    gather(n, g, s, [s_rows[n][s]])
                with pool.Fori(0, PAIRS) as i:
                    for s in (0, 1):
                        loads = held(pool, i * LOADS + LOADS * (n * PER_SLOT + 1))
                        table_ready()
                        pool.wait_ge(s_loaded[s], loads)
                        gather(n, None, s, [s_rows[n][s]])
                gather_group(FULL - 1, 0)
                gather_group(FULL, 1)

                pool.wait_ge(s_flag, 1)
                outside_any = pool.value_load(flag[0:1, 0:1], min_val=0, max_val=P)
                with pool.If(outside_any > 0):
                    with pool.Fori(0, FULL) as g:
                        loads = held(pool, g * LOADS + LOADS)
                        table_ready()
                        pool.wait_ge(r_loaded[n], loads)
                        gather(n, None, 0, r_rows[n])
                    pool.wait_ge(r_loaded[n], NG * LOADS)
                    gather(n, FULL, 0, r_rows[n])

        @block.scalar
        def _(act):
            act.wait_ge(s_iota, 1)
            nc.scalar.activation(iota[:, :], iota_sb[:, :], ACT.Copy).then_inc(s_iota, 1)
            act.wait_ge(s_mem, 3)

            def weight_column(g, s, uses):
                p, c = shape_of(g)
                act.wait_ge(s_loaded[s], uses)
                nc.scalar.activation(rows[s][0:p, 0:c, D + 1], weight[s][0:p, 0:c], ACT.Copy).then_inc(s_wcol, 1)
            with act.Fori(0, PAIRS) as i:
                weight_column(None, 0, i * LOADS + LOADS)
                weight_column(None, 1, i * LOADS + LOADS)
            weight_column(FULL - 1, 0, PER_SLOT * LOADS)
            weight_column(FULL, 1, PER_SLOT * LOADS)

            for n in range(4):
                act.wait_ge(s_added, (n + 1) * NG)
                act.wait_ge(s_flag, 1)
                outside_any = act.value_load(flag[0:1, 0:1], min_val=0, max_val=P)
                with act.If(outside_any > 0):
                    act.wait_ge(r_added[n], NG * TILES)
                height = SR if n == EDGE else D
                turned = n != NORM
                if n == EDGE:
                    act.wait_ge(s_nodes, 32)

                def stage(b, s):
                    nc.scalar.activation(sums_b[s][0:height, :], sums[0:height, bass.ds(b * BATCH, BATCH)],
                                         ACT.Copy).then_inc(s_staged[n], 1)
                    if turned:
                        nc.scalar.activation(nodes_b[s][:, :, :], nodes[:, bass.ds(b * TB, TB), :],
                                             ACT.Copy).then_inc(s_staged[n], 1)

                def roots(b, s):
                    if n in (EDGE, GCN):
                        act.wait_ge(s_turned[n], b + 1)
                        nc.scalar.activation(feats_b[s][:, :], feats_ps[:, 0:BATCH], ACT.Copy).then_inc(s_feats[n], 1)
                    if n == EDGE:
                        act.wait_ge(s_root_in[n], b * 2 + 1)
                        nc.scalar.activation(small[:, 3, :], small[:, 2, :], ACT.Sqrt).then_inc(s_root[n], 1)
                    if n == GCN:
                        act.wait_ge(s_root_in[n], b * 2 + 1)
                        nc.scalar.activation(work2[:, :, :], work[:, :, :], ACT.Tanh).then_inc(s_root[n], 1)
                    act.wait_ge(s_root_in[n], b * ROOTS[n] + ROOTS[n])
                    nc.scalar.activation(small[:, 7, 0:TB], small[:, 6, 0:TB], ACT.Sqrt).then_inc(s_root[n], 1)

                stage(0, 0)
                with act.Fori(0, NB // 2 - 1) as i:
                    stage(2 * i + 1, 1)
                    roots(2 * i, 0)
                    stage(2 * i + 2, 0)
                    roots(2 * i + 1, 1)
                stage(NB - 1, 1)
                roots(NB - 2, 0)
                roots(NB - 1, 1)

        @block.vector
        def _(dve):
            chain = Chain(dve, s_chain)
            nc.vector.memset(nodes[:, TILES - 1, :], 0.0).then_inc(s_mem, 1)
            for s in (0, 1):
                nc.vector.memset(rows[s][:, :, D:D + 1], 1.0).then_inc(s_mem, 1)
            nc.vector.memset(top[:, :], 0.0).then_inc(s_spread, 1)
            nc.vector.memset(low[:, :], 0.0).then_inc(s_spread, 1)
            nc.vector.memset(ones[:, :], 1.0).then_inc(s_prep, 1)
            dve.wait_ge(s_const, 11 * 16)
            dve.wait_ge(s_ident, 2)
            nc.vector.tensor_tensor(w0_own[:, :], w0_sb[:, 0, :], w0_sb[:, 1, :], ALU.subtract).then_inc(s_prep, 1)
            nc.vector.tensor_copy(w0_sums[:, :], ident[0:SR, 0:SR]).then_inc(s_prep, 1)
            dve.wait_ge(s_prep, 3)
            nc.vector.tensor_copy(w0_sums[0:D, 0:D], w0_sb[:, 1, :]).then_inc(s_prep, 1)
            dve.wait_ge(s_iota, 2)

            def turn_to_match(n, g, s, offsets, equal, matched, count):
                p, c = shape_of(g)
                nc.vector.tensor_tensor(match[s][0:p, 0:c, :],
                                        iota[0:p, :].unsqueeze(1).to_broadcast([p, c, P]),
                                        offsets[0:p, 0:c].unsqueeze(2).to_broadcast([p, c, P]),
                                        ALU.is_equal).then_inc(equal if WEIGHTED[n] else matched, 1)
                if WEIGHTED[n]:
                    dve.wait_ge(equal, count)
                    nc.vector.tensor_tensor(match[s][0:p, 0:c, :], match[s][0:p, 0:c, :],
                                            weight[s][0:p, 0:c].unsqueeze(2).to_broadcast([p, c, P]),
                                            ALU.mult).then_inc(matched, 1)

            for n in range(4):
                height = SR if n == EDGE else D
                if n:
                    dve.wait_ge(s_staged[n - 1], NB * (1 if n - 1 == NORM else 2))
                nc.vector.memset(sums[0:height, :], 0.0).then_inc(s_cleared, 1)
                weighted_before = sum(WEIGHTED[:n]) * NG

                def build_match(g, s, loads):
                    p, c = shape_of(g)
                    at = g + n * NG
                    dve.wait_ge(s_loaded[s], loads)
                    nc.vector.tensor_scalar(offset[s][0:p, 0:c], dst_ix[s][0:p, 0:c], first[s][0:p, 0:1], None,
                                            ALU.subtract).then_inc(s_offset, 1)
                    dve.wait_ge(s_offset, at + 1)
                    if n == EDGE:
                        dve.wait_ge(s_spread, 2 * g + 2)
                        nc.vector.tensor_tensor(top[0:p, 0:c], top[0:p, 0:c], offset[s][0:p, 0:c],
                                                ALU.max).then_inc(s_spread, 1)
                        nc.vector.tensor_tensor(low[0:p, 0:c], low[0:p, 0:c], offset[s][0:p, 0:c],
                                                ALU.min).then_inc(s_spread, 1)
                    turn_to_match(n, g, s, offset[s], s_equal, s_match, g + weighted_before + 1)

                def add_part(g, s):
                    at = g + n * NG
                    node = dve.value_load(first[s][0:1, 0:1], min_val=0, max_val=V - 1)
                    dve.wait_ge(s_part, at + 1)
                    dve.wait_ge(s_added, at) if not (isinstance(at, int) and at == 0) else None
                    nc.vector.tensor_tensor(sums[0:height, bass.ds(node, P)], sums[0:height, bass.ds(node, P)],
                                            part[s][0:height, :], ALU.add).then_inc(s_added, 1)

                before = n * PER_SLOT * LOADS
                build_match(0, 0, before + LOADS)
                dve.wait_ge(s_cleared, n + 1)
                with dve.Fori(0, PAIRS) as i:
                    build_match(2 * i + 1, 1, i * LOADS + before + LOADS)
                    add_part(2 * i, 0)
                    build_match(2 * i + 2, 0, i * LOADS + before + 2 * LOADS)
                    add_part(2 * i + 1, 1)
                build_match(FULL, 1, before + PER_SLOT * LOADS)
                add_part(FULL - 1, 0)
                add_part(FULL, 1)

                if n == EDGE:
                    dve.wait_ge(s_spread, 2 * NG + 2)
                    chain.step(nc.vector.tensor_reduce(spread[:, 0:1], top[:, :], AX.X, ALU.max))
                    chain.step(nc.vector.tensor_reduce(spread[:, 1:2], low[:, :], AX.X, ALU.min))
                    chain.step(nc.vector.tensor_scalar(spread[:, 2:3], spread[:, 0:1], float(P), None, ALU.is_ge))
                    chain.step(nc.vector.tensor_scalar(spread[:, 3:4], spread[:, 1:2], 0.0, None, ALU.is_lt))
                    nc.vector.tensor_tensor(spread[:, 2:3], spread[:, 2:3], spread[:, 3:4],
                                            ALU.max).then_inc(s_prep, 1)
                    dve.wait_ge(s_out_ps, 1)
                    nc.vector.tensor_copy(flag[0:1, 0:1], second_ps[0:1, 0, 0:1]).then_inc(s_flag, 1)
                dve.wait_ge(s_flag, 1)
                outside_any = dve.value_load(flag[0:1, 0:1], min_val=0, max_val=P)
                with dve.If(outside_any > 0):
                    def slow_group(g, done_groups):
                        p, c = shape_of(g)
                        per_window, head = SLOW[n]
                        base = done_groups * (head + TILES * per_window)
                        dve.wait_ge(r_loaded[n], done_groups * LOADS + LOADS)
                        steps = [
                            lambda: nc.vector.tensor_scalar(offset[0][0:p, 0:c], dst_ix[0][0:p, 0:c],
                                                            first[0][0:p, 0:1], None, ALU.subtract),
                            lambda: nc.vector.tensor_scalar(outside[0:p, 0:c, 0], offset[0][0:p, 0:c], 0.0, None,
                                                            ALU.is_ge),
                            lambda: nc.vector.scalar_tensor_tensor(outside[0:p, 0:c, 1], offset[0][0:p, 0:c],
                                                                   float(P), outside[0:p, 0:c, 0],
                                                                   ALU.is_lt, ALU.mult),
                            lambda: nc.vector.scalar_tensor_tensor(offset[1][0:p, 0:c], outside[0:p, 0:c, 1],
                                                                   float(2 * VP), dst_ix[0][0:p, 0:c],
                                                                   ALU.mult, ALU.add),
                        ]
                        if n == EDGE:
                            steps.append(lambda: nc.vector.tensor_copy(rows[0][0:p, 0:c, D + 1],
                                                                       weight[0][0:p, 0:c]))
                        for k, step in enumerate(steps):
                            step().then_inc(r_match[n], 1)
                            steps_done = held(dve, base + k + 1)
                            dve.wait_ge(s_flag, 1)
                            dve.wait_ge(r_match[n], steps_done)
                        with dve.Fori(0, TILES) as w:
                            now = w * per_window + base + head
                            nc.vector.tensor_tensor(match[0][0:p, 0:c, :],
                                                    iota[0:p, :].unsqueeze(1).to_broadcast([p, c, P]),
                                                    offset[1][0:p, 0:c].unsqueeze(2).to_broadcast([p, c, P]),
                                                    ALU.is_equal).then_inc(r_match[n], 1)
                            dve.wait_ge(r_match[n], now + 1)
                            if WEIGHTED[n]:
                                nc.vector.tensor_tensor(match[0][0:p, 0:c, :], match[0][0:p, 0:c, :],
                                                        weight[0][0:p, 0:c].unsqueeze(2).to_broadcast([p, c, P]),
                                                        ALU.mult).then_inc(r_match[n], 1)
                                dve.wait_ge(r_match[n], now + 2)
                            nc.vector.tensor_scalar(offset[1][0:p, 0:c], offset[1][0:p, 0:c], float(P), None,
                                                    ALU.subtract).then_inc(r_match[n], 1)
                            dve.wait_ge(r_part[n], w + done_groups * TILES + 1)
                            nc.vector.tensor_tensor(sums[0:height, bass.ds(w * P, P)],
                                                    sums[0:height, bass.ds(w * P, P)],
                                                    part[0][0:height, :], ALU.add).then_inc(r_added[n], 1)
                            dve.wait_ge(r_added[n], w + done_groups * TILES + 1)
                            dve.wait_ge(r_match[n], now + per_window)
                    with dve.Fori(0, FULL) as g:
                        slow_group(None, g)
                    slow_group(FULL, FULL)

                if n == EDGE:
                    dve.wait_ge(s_nodes, 32)

                def layer_norm(b, s):
                    own = nodes[:, bass.ds(b * TB, TB), :]
                    chain.step(nc.vector.tensor_reduce(small[:, 4, 0:TB], work[:, :, :], AX.X, ALU.add))
                    chain.step(nc.vector.tensor_scalar(small[:, 4, 0:TB], small[:, 4, 0:TB], 1.0 / D, None, ALU.mult))
                    chain.step(nc.vector.tensor_tensor(work[:, :, :], work[:, :, :],
                                                       small[:, 4, 0:TB].unsqueeze(2).to_broadcast([P, TB, D]),
                                                       ALU.subtract))
                    chain.step(nc.vector.tensor_tensor(work2[:, :, :], work[:, :, :], work[:, :, :], ALU.mult))
                    chain.step(nc.vector.tensor_reduce(small[:, 5, 0:TB], work2[:, :, :], AX.X, ALU.add))
                    chain.step(nc.vector.tensor_scalar(small[:, 5, 0:TB], small[:, 5, 0:TB], 1.0 / D, EPS,
                                                       ALU.mult, ALU.add))
                    nc.vector.reciprocal(small[:, 6, 0:TB], small[:, 5, 0:TB]).then_inc(s_root_in[n], 1)
                    dve.wait_ge(s_root[n], b * ROOTS[n] + ROOTS[n])
                    rstd = small[:, 7, 0:TB].unsqueeze(2).to_broadcast([P, TB, D])
                    if n == BI:
                        last = nc.vector.tensor_tensor(result[s][:, :, :], work[:, :, :], rstd, ALU.mult)
                    else:
                        chain.step(nc.vector.tensor_tensor(own, work[:, :, :], rstd, ALU.mult))
                        if n == NORM:
                            last = nc.vector.tensor_tensor(result[s][:, :, :], work[:, :, :], rstd, ALU.mult)
                        else:
                            scale = gcn_scale if n == EDGE else norm_scale
                            last = nc.vector.tensor_tensor(
                                result[s][:, :, :], own,
                                scale[:, bass.ds(b * TB, TB)].unsqueeze(2).to_broadcast([P, TB, D]), ALU.mult)
                    last.then_inc(s_result[n], 1)
                    dve.wait_ge(s_result[n], b + 1)

                def spread_bias(k):
                    return bias[:, k, :].unsqueeze(1).to_broadcast([P, TB, D])

                def batch(b, s, turn):
                    own = nodes[:, bass.ds(b * TB, TB), :]
                    if n == BI:
                        dve.wait_ge(s_turned[n], b + 1)
                        nc.vector.tensor_tensor(feats_b[s][:, :], feats_ps[:, 0:BATCH], sums_b[s][0:D, :],
                                                ALU.add).then_inc(s_feats[n], 1)
                        nc.vector.tensor_tensor(prod_b[s][:, :], feats_ps[:, 0:BATCH], sums_b[s][0:D, :],
                                                ALU.mult).then_inc(s_feats[n], 1)
                    dve.wait_ge(s_prods[n], b + 1)
                    if turn is not None:
                        dve.wait_ge(s_stored[n][s], turn * 16)
                    msg = first_ps[:, :, 0:D]
                    if n == EDGE:
                        count, degree = first_ps[:, :, D], first_ps[:, :, D + 1]
                        chain.step(nc.vector.tensor_scalar(small[:, 0, 0:TB], count, 1.0, None, ALU.max))
                        chain.step(nc.vector.tensor_scalar(small[:, 1, TB:2 * TB], degree, FILL, None, ALU.add))
                        chain.step(nc.vector.tensor_scalar(small[:, 0, TB:2 * TB], small[:, 1, TB:2 * TB], 1e-30, None,
                                                           ALU.max))
                        chain.step(nc.vector.tensor_scalar(small[:, 4, TB:2 * TB], small[:, 1, TB:2 * TB], 0.0, None,
                                                           ALU.is_gt))
                        nc.vector.reciprocal(small[:, 2, :], small[:, 0, :]).then_inc(s_root_in[n], 1)
                        chain.step(nc.vector.tensor_scalar(small[:, 4, 0:TB], count, 0.0, None, ALU.is_gt))
                        dve.wait_ge(s_root_in[n], b * 2 + 1)
                        chain.step(nc.vector.tensor_tensor(work[:, :, :], msg,
                                                           small[:, 2, 0:TB].unsqueeze(2).to_broadcast([P, TB, D]),
                                                           ALU.mult))
                        nc.vector.tensor_tensor(work2[:, :, :], work[:, :, :], second_ps[:, :, :],
                                                ALU.add).then_inc(s_taken[n], 1)
                        dve.wait_ge(s_taken[n], b + 1)
                        chain.step(nc.vector.tensor_tensor(work2[:, :, :], work2[:, :, :], spread_bias(0), ALU.add))
                        chain.step(nc.vector.tensor_tensor(work2[:, :, :], work2[:, :, :],
                                                           small[:, 4, 0:TB].unsqueeze(2).to_broadcast([P, TB, D]),
                                                           ALU.mult))
                        chain.step(nc.vector.tensor_tensor(work[:, :, :], work2[:, :, :], own, ALU.add))
                        dve.wait_ge(s_root[n], b * 2 + 1)
                        chain.step(nc.vector.reciprocal(small[:, 5, :], small[:, 3, :]))
                        chain.step(nc.vector.tensor_tensor(small[:, 5, :], small[:, 5, :], small[:, 2, :], ALU.mult))
                        chain.step(nc.vector.tensor_tensor(small[:, 5, :], small[:, 5, :], small[:, 3, :], ALU.add))
                        chain.step(nc.vector.tensor_scalar(small[:, 5, :], small[:, 5, :], 0.5, None, ALU.mult))
                        chain.step(nc.vector.tensor_copy(norm_scale[:, bass.ds(b * TB, TB)], small[:, 5, 0:TB]))
                        chain.step(nc.vector.tensor_tensor(gcn_scale[:, bass.ds(b * TB, TB)], small[:, 5, TB:2 * TB],
                                                           small[:, 4, TB:2 * TB], ALU.mult))
                        chain.step(nc.vector.tensor_scalar(small[:, 5, 0:TB], gcn_scale[:, bass.ds(b * TB, TB)],
                                                           FILL, None, ALU.mult))
                        chain.step(nc.vector.tensor_tensor(gcn_loop[:, bass.ds(b * TB, TB)],
                                                           gcn_scale[:, bass.ds(b * TB, TB)], small[:, 5, 0:TB],
                                                           ALU.mult))
                    if n == GCN:
                        chain.step(nc.vector.tensor_tensor(
                            work[:, :, :], msg,
                            gcn_scale[:, bass.ds(b * TB, TB)].unsqueeze(2).to_broadcast([P, TB, D]), ALU.mult))
                        nc.vector.tensor_tensor(
                            work2[:, :, :], second_ps[:, :, :],
                            gcn_loop[:, bass.ds(b * TB, TB)].unsqueeze(2).to_broadcast([P, TB, D]),
                            ALU.mult).then_inc(s_taken[n], 1)
                        dve.wait_ge(s_taken[n], b + 1)
                        chain.step(nc.vector.tensor_tensor(work[:, :, :], work[:, :, :], work2[:, :, :], ALU.add))
                        nc.vector.tensor_tensor(work[:, :, :], work[:, :, :], spread_bias(1),
                                                ALU.add).then_inc(s_root_in[n], 1)
                        dve.wait_ge(s_root[n], b * 2 + 1)
                        chain.step(nc.vector.tensor_tensor(work[:, :, :], work2[:, :, :], own, ALU.add))
                    if n == NORM:
                        nc.vector.tensor_tensor(
                            work[:, :, :], msg,
                            norm_scale[:, bass.ds(b * TB, TB)].unsqueeze(2).to_broadcast([P, TB, D]),
                            ALU.mult).then_inc(s_taken[n], 1)
                        dve.wait_ge(s_taken[n], b + 1)
                        chain.step(nc.vector.tensor_tensor(work[:, :, :], work[:, :, :], spread_bias(2), ALU.add))
                        chain.step(nc.vector.tensor_tensor(work[:, :, :], work[:, :, :], own, ALU.add))
                    if n == BI:
                        chain.step(nc.vector.tensor_tensor(work[:, :, :], msg, spread_bias(3), ALU.add))
                        nc.vector.tensor_tensor(work2[:, :, :], second_ps[:, :, :], spread_bias(4),
                                                ALU.add).then_inc(s_taken[n], 1)
                        chain.step(nc.vector.scalar_tensor_tensor(work[:, :, :], work[:, :, :], SLOPE, work[:, :, :],
                                                                  ALU.mult, ALU.max))
                        dve.wait_ge(s_taken[n], b + 1)
                        chain.step(nc.vector.scalar_tensor_tensor(work2[:, :, :], work2[:, :, :], SLOPE,
                                                                  work2[:, :, :], ALU.mult, ALU.max))
                        chain.step(nc.vector.tensor_tensor(work[:, :, :], work[:, :, :], work2[:, :, :], ALU.add))
                        chain.step(nc.vector.tensor_tensor(work[:, :, :], work[:, :, :], own, ALU.add))
                    layer_norm(b, s)

                each = {EDGE: 17 + 7, GCN: 3 + 7, NORM: 2 + 7, BI: 5 + 6}[n]
                chain.enter(0, 0)
                batch(0, 0, None)
                batch(1, 1, None)
                assert chain.k == 2 * each, (n, chain.k, each)
                with dve.Fori(1, NB // 2) as i:
                    chain.enter(i - 1, 2 * each)
                    batch(2 * i, 0, i)
                    batch(2 * i + 1, 1, i)
                chain.leave(NB // 2 - 1)

        @block.tensor
        def _(pe):
            def sum_by_node(n, g, s, done):
                p, c = shape_of(g)
                height = SR if n == EDGE else D
                for j in range(c):
                    last = nc.tensor.matmul(part[s][0:height, :], rows[s][0:p, j, 0:height], match[s][0:p, j, :],
                                            start=(j == 0), stop=(j == c - 1))
                last.then_inc(done, 1)

            for n in range(4):
                def sum_group(g, s, rows_in):
                    at = g + n * NG
                    pe.wait_ge(s_rows[n][s], rows_in)
                    pe.wait_ge(s_match, at + 1)
                    if n == EDGE:
                        pe.wait_ge(s_wcol, at + 1)
                    sum_by_node(n, g, s, s_part)
                ROWS = CHUNKS * 16
                with pe.Fori(0, PAIRS) as i:
                    sum_group(2 * i, 0, i * ROWS + ROWS)
                    sum_group(2 * i + 1, 1, i * ROWS + ROWS)
                sum_group(FULL - 1, 0, PER_SLOT * ROWS)
                sum_group(FULL, 1, (PER_SLOT - 1) * ROWS + TAIL_C * 16)

                if n == EDGE:
                    pe.wait_ge(s_prep, 5)
                    nc.tensor.matmul(second_ps[0:1, 0, 0:1], spread[:, 2:3], ones[:, 0:1], start=True,
                                     stop=True).then_inc(s_out_ps, 1)
                pe.wait_ge(s_flag, 1)
                outside_any = pe.value_load(flag[0:1, 0:1], min_val=0, max_val=P)
                with pe.If(outside_any > 0):
                    per_window, head = SLOW[n]

                    def slow_group(g, done_groups, rows_in):
                        rows_held = [held(pe, v) for v in rows_in]
                        pe.wait_ge(s_flag, 1)
                        for j in (0, 1):
                            pe.wait_ge(r_rows[n][j], rows_held[j])
                        with pe.Fori(0, TILES) as w:
                            pe.wait_ge(r_match[n], w * per_window + done_groups * (head + TILES * per_window)
                                       + head + per_window)
                            sum_by_node(n, g, 0, r_part[n])
                    half = CHUNKS // 2 * 16
                    with pe.Fori(0, FULL) as g:
                        slow_group(None, g, [g * half + half] * 2)
                    slow_group(FULL, FULL, [FULL * half + (TAIL_C + 1) // 2 * 16, FULL * half + TAIL_C // 2 * 16])

                height = SR if n == EDGE else D
                per_stage = 1 if n == NORM else 2
                pe.wait_ge(s_prep, 5)

                def turn_nodes(b, s, waits):
                    staged, read = held(pe, b * 2 + 2), held(pe, b * (2 if n == BI else 1))
                    pe.wait_ge(s_ident, 2)
                    pe.wait_ge(s_staged[n], staged)
                    if waits:
                        pe.wait_ge(s_feats[n], read)
                    for t in range(TB):
                        last = nc.tensor.transpose(feats_ps[:, t * P:(t + 1) * P], nodes_b[s][:, t, :], ident[:, :])
                    last.then_inc(s_turned[n], 1)

                def products(b, s, waits):
                    if n == NORM:
                        pe.wait_ge(s_staged[n], b + 1)
                    else:
                        pe.wait_ge(s_feats[n], b * (2 if n == BI else 1) + (2 if n == BI else 1))
                    if waits:
                        pe.wait_ge(s_taken[n], b)
                    first_w = (w0_sums[:, :], w1_sb[:, :], w2_sb[:, :], w_gc_sb[:, :])[n]
                    second_w = (w0_own[:, :], w1_sb[:, :], None, w_bi_sb[:, :])[n]
                    first_in = feats_b[s] if n == BI else sums_b[s]
                    second_in = prod_b[s] if n == BI else feats_b[s]
                    for t in range(TB):
                        last = nc.tensor.matmul(first_ps[:, t, 0:height], first_in[0:height, t * P:(t + 1) * P],
                                                first_w, start=True, stop=True)
                        if second_w is not None:
                            last = nc.tensor.matmul(second_ps[:, t, :], second_in[:, t * P:(t + 1) * P],
                                                    second_w, start=True, stop=True)
                    last.then_inc(s_prods[n], 1)

                def batch(b, s, waits):
                    if n != NORM:
                        turn_nodes(b, s, waits)
                    products(b, s, waits)
                batch(0, 0, False)
                batch(1, 1, True)
                with pe.Fori(1, NB // 2) as i:
                    batch(2 * i, 0, True)
                    batch(2 * i + 1, 1, True)


_INS = ['x', 'src', 'dst', 'edge_weight', 'L0_gnn_W', 'L0_gnn_b', 'L1_gnn_W', 'L1_gnn_b', 'L2_gnn_weight',
        'L2_gnn_bias', 'L3_gnn_W_gc', 'L3_gnn_b_gc', 'L3_gnn_W_bi', 'L3_gnn_b_bi']


def kernel(**inputs):
    import numpy as _np
    import concourse.bacc as _bacc
    from concourse import mybir as _mybir
    from concourse.bass_utils import run_bass_kernel_spmd as _run

    nc = _bacc.Bacc("TRN2", target_bir_lowering=False, num_devices=1)
    arrays, args = {}, []
    for name in _INS:
        a = _np.ascontiguousarray(inputs[name])
        arrays[f"in_{name}_dram"] = a
        args.append(nc.dram_tensor(f"in_{name}_dram", a.shape, _mybir.dt.from_np(a.dtype), kind="ExternalInput").ap())
    out = nc.dram_tensor("out_0_dram", arrays["in_x_dram"].shape, _mybir.dt.float32, kind="ExternalOutput").ap()
    build(nc, *args, out)
    r = _run(nc, [arrays], core_ids=[0])
    return r.results[0]["out_0_dram"]
```

```python
import concourse.bass as bass
from concourse import mybir
from contextlib import ExitStack

F32 = mybir.dt.float32
I32 = mybir.dt.int32
U32 = mybir.dt.uint32
ALU = mybir.AluOpType
ACT = mybir.ActivationFunctionType
AX = mybir.AxisListType

P = 128
CHUNKS = 16
EDGE, GCN, NORM, BI = range(4)
WEIGHTED = (False, True, False, True)
EPS = 1e-5
SLOPE = 0.01
FILL = 2.0


def held(engine, value):
    return value if isinstance(value, int) else engine.to_reg(value)


class Chain:

    def __init__(self, engine, sem):
        self.engine, self.sem, self.start, self.k = engine, sem, 0, 0

    def begin(self, start):
        self.start, self.k = start, 0

    def step(self, instruction):
        self.k += 1
        instruction.then_inc(self.sem, 1)
        self.engine.wait_ge(self.sem, self.start + self.k)


def build(nc, x, src, dst, edge_weight, w0, b0, w1, b1, w2, b2, w_gc, b_gc, w_bi, b_bi, out):
    V, D = x.shape
    E = src.shape[0]
    GROUP = P * CHUNKS
    FULL = E // GROUP
    REST = E - FULL * GROUP
    TAIL_C = max(c for c in range(1, CHUNKS + 1) if REST % c == 0 and REST // c <= P)
    TAIL_P = REST // TAIL_C
    assert REST and TAIL_P <= P and FULL % 2 == 1
    NG = FULL + 1
    PAIRS = (FULL - 1) // 2
    TILES = -(-V // P)
    TB = 7
    NB = TILES // TB
    assert TILES == NB * TB
    VP = TILES * P
    BATCH = TB * P
    DUE = E / GROUP * BATCH / V
    EVERY = int(DUE) // 2
    AHEAD = int(-(-(DUE * (NB - 1) + 1 - 2 * EVERY * (NB - 2)) // 2))
    AFTER = PAIRS - AHEAD - EVERY * (NB - 2)
    PIECES = 4
    assert EVERY >= PIECES and AFTER >= PIECES and AHEAD >= 1
    SR = D + 2

    tables = [x] + [nc.dram_tensor(f"table_{n}", (VP, D), F32, kind="Internal").ap() for n in (GCN, NORM, BI)]
    biases = (b0, b1, b2, b_gc, b_bi)

    with ExitStack() as ctx:
        def sb(name, shape, dt=F32):
            return ctx.enter_context(nc.sbuf_tensor(name, shape, dt))

        def ps(name, shape):
            return ctx.enter_context(nc.psum_tensor(name, shape, F32))

        def sem(name):
            return ctx.enter_context(nc.semaphore(name))

        src_ix = [sb(f"src_ix{s}", [P, CHUNKS], U32) for s in (0, 1)]
        dst_ix = [sb(f"dst_ix{s}", [P, CHUNKS], I32) for s in (0, 1)]
        weight = [sb(f"weight{s}", [P, CHUNKS]) for s in (0, 1)]
        first = [sb(f"first{s}", [P, 1], I32) for s in (0, 1)]
        offset = [sb(f"offset{s}", [P, CHUNKS]) for s in (0, 1)]
        match = [sb(f"match{s}", [P, CHUNKS, P]) for s in (0, 1)]
        rows = [sb(f"rows{s}", [P, CHUNKS, SR]) for s in (0, 1)]
        part = [ps(f"part{s}", [SR, P]) for s in (0, 1)]
        sums = sb("sums", [SR, VP + P])
        nodes = [sb(f"nodes{s}", [P, TILES, D]) for s in (0, 1)]
        gcn_scale = sb("gcn_scale", [P, TILES])
        gcn_loop = sb("gcn_loop", [P, TILES])
        norm_scale = sb("norm_scale", [P, TILES])
        sums_b = sb("sums_b", [SR, BATCH])
        nodes_b = sb("nodes_b", [P, TB, D])
        feats_b = sb("feats_b", [D, BATCH])
        prod_b = sb("prod_b", [D, BATCH])
        result = sb("result", [P, TB, D])
        work = sb("work", [P, TB, D])
        work2 = sb("work2", [P, TB, D])
        small = sb("small", [P, 8, 2 * TB])
        feats_ps = ps("feats_ps", [D, 1024])
        first_ps = ps("first_ps", [P, TB, SR])
        second_ps = ps("second_ps", [P, TB, D])
        ident = sb("ident", [P, P])
        iota_sb = sb("iota_sb", [P, P])
        iota = ps("iota", [P, P])
        ones = sb("ones", [P, 1])
        bias = sb("bias", [P, len(biases), D])
        w0_sb = sb("w0_sb", [D, 2, D])
        w0_own = sb("w0_own", [D, D])
        w0_sums = sb("w0_sums", [SR, SR])
        w1_sb = sb("w1_sb", [D, D])
        w2_sb = sb("w2_sb", [D, D])
        w_gc_sb = sb("w_gc_sb", [D, D])
        w_bi_sb = sb("w_bi_sb", [D, D])
        top = sb("top", [P, CHUNKS])
        low = sb("low", [P, CHUNKS])
        limit = sb("limit", [P, 1])
        ahead = sb("ahead", [P, 2])
        spread = sb("spread", [P, 4])
        flag = sb("flag", [1, 1], I32)
        outside = sb("outside", [P, CHUNKS, 2])

        s_loaded = [sem(f"s_loaded{s}") for s in (0, 1)]
        s_rows = [[sem(f"s_rows{n}_{s}") for s in (0, 1)] for n in range(4)]
        s_wcol = sem("s_wcol")
        s_offset = sem("s_offset")
        s_spread = sem("s_spread")
        s_equal = sem("s_equal")
        s_match = sem("s_match")
        s_part = sem("s_part")
        s_added = sem("s_added")
        s_cleared = sem("s_cleared")
        s_flag = sem("s_flag")
        s_out_ps = sem("s_out_ps")
        s_const = sem("s_const")
        s_nodes = sem("s_nodes")
        s_mem = sem("s_mem")
        s_ident = sem("s_ident")
        s_iota = sem("s_iota")
        s_prep = sem("s_prep")
        s_chain = sem("s_chain")
        s_limit = sem("s_limit")
        class Batches:
            def __init__(self, name):
                self.staged = sem(f"{name}_staged")
                self.turned = sem(f"{name}_turned")
                self.feats = sem(f"{name}_feats")
                self.prods = sem(f"{name}_prods")
                self.taken = sem(f"{name}_taken")
                self.root_in = sem(f"{name}_root_in")
                self.root = sem(f"{name}_root")
                self.result = sem(f"{name}_result")
                self.stored = sem(f"{name}_stored")
        timely = [Batches(f"s{n}") for n in range(4)]
        again = [Batches(f"a{n}") for n in range(4)]
        r_loaded = [sem(f"r_loaded{n}") for n in range(4)]
        r_rows = [[sem(f"r_rows{n}_{j}") for j in (0, 1)] for n in range(4)]
        r_match = [sem(f"r_match{n}") for n in range(4)]
        r_part = [sem(f"r_part{n}") for n in range(4)]
        r_added = [sem(f"r_added{n}") for n in range(4)]
        r_chain = sem("r_chain")

        block = ctx.enter_context(nc.Block())

        def shape_of(g):
            return (TAIL_P, TAIL_C) if isinstance(g, int) and g == FULL else (P, CHUNKS)

        def edges_of(array, g):
            p, c = shape_of(g)
            return array[bass.ds(g * GROUP, p * c)].rearrange("(p c) -> p c", c=c)

        def load_group(sp, g, s, loaded):
            p, c = shape_of(g)
            sp.dma_start(src_ix[s][0:p, 0:c].bitcast(I32), edges_of(src, g)).then_inc(loaded, 16)
            sp.dma_start(dst_ix[s][0:p, 0:c], edges_of(dst, g)).then_inc(loaded, 16)
            sp.dma_start(weight[s][0:p, 0:c], edges_of(edge_weight, g)).then_inc(loaded, 16)
            sp.dma_start(first[s][:, :], dst[bass.ds(g * GROUP, 1)].partition_broadcast(P)).then_inc(loaded, 16)

        LOADS = 4 * 16
        PER_SLOT = NG // 2

        def stored_all(n):
            return 16 * (NB + (n == BI))

        def with_batches(engine, pair, batch, pieces=PIECES):
            def one(b, first_pair, pairs):
                share = batch(b)
                for k in range(pieces):
                    next(share, None)
                    pair(first_pair + k)
                if pairs > pieces:
                    with engine.Fori(0, pairs - pieces) as i:
                        pair(i + first_pair + pieces)
            with engine.Fori(0, AHEAD) as i:
                pair(i)
            with engine.Fori(0, NB - 2) as b:
                one(b, b * EVERY + AHEAD, EVERY)
            one(NB - 2, AHEAD + EVERY * (NB - 2), AFTER)

        ROOTS = (2, 2, 1, 1)
        SLOW = ((2, 5), (3, 4), (2, 4), (3, 4))

        @block.sync
        def _(sp):
            full_tiles = V // P
            with nc.allow_non_contiguous_dma(reason="weights are transposed and biases repeated once"):
                for n in range(4):
                    def load(g, s):
                        if not (isinstance(g, int) and n * NG + g < 2):
                            sp.wait_ge(s_added, n * NG - 1 + g)
                        load_group(sp, g, s, s_loaded[s])
                    load(0, 0)
                    load(1, 1)
                    if n == 0:
                        sp.dma_start(w0_sb[:, 0, :], w0[:, 0:D].rearrange("o c -> c o")).then_inc(s_const, 16)
                        sp.dma_start(w0_sb[:, 1, :], w0[:, D:2 * D].rearrange("o c -> c o")).then_inc(s_const, 16)
                        sp.dma_start(w1_sb[:, :], w1).then_inc(s_const, 16)
                        sp.dma_start(w2_sb[:, :], w2).then_inc(s_const, 16)
                        sp.dma_start(w_gc_sb[:, :], w_gc.rearrange("o c -> c o")).then_inc(s_const, 16)
                        sp.dma_start(w_bi_sb[:, :], w_bi.rearrange("o c -> c o")).then_inc(s_const, 16)
                        for k, b in enumerate(biases):
                            sp.dma_start(bias[:, k, :], b.partition_broadcast(P)).then_inc(s_const, 16)
                        sp.wait_ge(s_mem, 1)
                        sp.dma_start(nodes[0][:, 0:full_tiles, :],
                                     x[0:full_tiles * P, :].rearrange("(t p) f -> p t f", p=P)).then_inc(s_nodes, 16)
                        sp.dma_start(nodes[0][0:V - full_tiles * P, full_tiles, :],
                                     x[full_tiles * P:V, :]).then_inc(s_nodes, 16)
                    with sp.Fori(1, PAIRS) as i:
                        load(2 * i, 0)
                        load(2 * i + 1, 1)
                    load(FULL - 1, 0)
                    load(FULL, 1)

                    sp.wait_ge(s_flag, 1)
                    outside_any = sp.value_load(flag[0:1, 0:1], min_val=0, max_val=P)
                    with sp.If(outside_any > 0):
                        def reload(g, done):
                            sp.wait_ge(r_added[n], done)
                            load_group(sp, g, 0, r_loaded[n])
                        sp.wait_ge(s_added, (n + 1) * NG)
                        load_group(sp, 0, 0, r_loaded[n])
                        with sp.Fori(1, FULL) as g:
                            reload(g, g * TILES)
                        reload(FULL, FULL * TILES)
                        sp.wait_ge(r_added[n], NG * TILES)

        @block.gpsimd
        def _(pool):
            nc.gpsimd.memset(ident[:, :], 0.0).then_inc(s_ident, 1)
            nc.gpsimd.iota(iota_sb[:, :], pattern=[[1, P]], base=0, channel_multiplier=0,
                           allow_small_or_imprecise_dtypes=True).then_inc(s_iota, 1)
            pool.wait_ge(s_ident, 1)
            nc.gpsimd.affine_select(out=ident[:, :], in_=ident[:, :], compare_op=ALU.not_equal, fill=1.0,
                                    base=0, pattern=[[-1, P]], channel_multiplier=1).then_inc(s_ident, 1)

            def gather(n, g, s, sems):
                p, c = shape_of(g)
                for j in range(c):
                    pool.indirect_dma_start(
                        rows[s][0:p, j, 0:D], None, tables[n][:, :],
                        bass.IndirectOffsetOnAxis(ap=src_ix[s][0:p, j:j + 1], axis=0),
                    ).then_inc(sems[j % len(sems)], 16)

            for n in range(4):
                def table_ready():
                    if n:
                        pool.wait_ge(timely[n - 1].stored, stored_all(n - 1))
                    else:
                        pool.wait_ge(s_ident, 2)

                def gather_group(g, s):
                    table_ready()
                    pool.wait_ge(s_loaded[s], LOADS * (n + 1) * PER_SLOT)
                    gather(n, g, s, [s_rows[n][s]])
                with pool.Fori(0, PAIRS) as i:
                    for s in (0, 1):
                        loads = held(pool, i * LOADS + LOADS * (n * PER_SLOT + 1))
                        table_ready()
                        pool.wait_ge(s_loaded[s], loads)
                        gather(n, None, s, [s_rows[n][s]])
                gather_group(FULL - 1, 0)
                gather_group(FULL, 1)

                pool.wait_ge(s_flag, 1)
                outside_any = pool.value_load(flag[0:1, 0:1], min_val=0, max_val=P)
                with pool.If(outside_any > 0):
                    with pool.Fori(0, FULL) as g:
                        loads = held(pool, g * LOADS + LOADS)
                        table_ready()
                        pool.wait_ge(r_loaded[n], loads)
                        gather(n, None, 0, r_rows[n])
                    pool.wait_ge(r_loaded[n], NG * LOADS)
                    gather(n, FULL, 0, r_rows[n])
                    pool.wait_ge(again[n].stored, stored_all(n))

        @block.scalar
        def _(act):
            act.wait_ge(s_iota, 1)
            nc.scalar.activation(iota[:, :], iota_sb[:, :], ACT.Copy).then_inc(s_iota, 1)
            act.wait_ge(s_mem, 3)

            def weight_column(g, s, uses):
                p, c = shape_of(g)
                act.wait_ge(s_loaded[s], uses)
                nc.scalar.activation(rows[s][0:p, 0:c, D + 1], weight[s][0:p, 0:c], ACT.Copy).then_inc(s_wcol, 1)

            for n in range(4):
                height = SR if n == EDGE else D

                def batch(b, at):
                    nc.scalar.activation(sums_b[0:height, :], sums[0:height, bass.ds(b * BATCH, BATCH)],
                                         ACT.Copy).then_inc(at.staged, 1)
                    if n != NORM:
                        nc.scalar.activation(nodes_b[:, :, :], nodes[n % 2][:, bass.ds(b * TB, TB), :],
                                             ACT.Copy).then_inc(at.staged, 1)
                    if n in (EDGE, GCN):
                        act.wait_ge(at.turned, b + 1)
                        nc.scalar.activation(feats_b[:, :], feats_ps[:, 0:BATCH], ACT.Copy).then_inc(at.feats, 1)
                    yield
                    if n == EDGE:
                        act.wait_ge(at.root_in, b * 2 + 1)
                        nc.scalar.activation(small[:, 3, :], small[:, 2, :], ACT.Sqrt).then_inc(at.root, 1)
                    if n == GCN:
                        act.wait_ge(at.root_in, b * 2 + 1)
                        nc.scalar.activation(work2[:, :, :], work[:, :, :], ACT.Tanh).then_inc(at.root, 1)
                    yield
                    act.wait_ge(at.root_in, b * ROOTS[n] + ROOTS[n])
                    nc.scalar.activation(small[:, 7, 0:TB], small[:, 6, 0:TB], ACT.Sqrt).then_inc(at.root, 1)
                    yield
                    to = out if n == BI else tables[n + 1]
                    act.wait_ge(at.result, b + 1)
                    if n == BI and isinstance(b, int) and b == NB - 1:
                        start = b * BATCH
                        whole = (V - start) // P
                        act.dma_start(to[start:start + whole * P, :].rearrange("(t p) f -> p t f", p=P),
                                      result[:, 0:whole, :]).then_inc(at.stored, 16)
                        act.dma_start(to[start + whole * P:V, :],
                                      result[0:V - start - whole * P, whole, :]).then_inc(at.stored, 16)
                    else:
                        act.dma_start(to[bass.ds(b * BATCH, BATCH), :].rearrange("(t p) f -> p t f", p=P),
                                      result[:, :, :]).then_inc(at.stored, 16)

                def pair(i):
                    if n == EDGE:
                        for s in (0, 1):
                            weight_column(None, s, i * LOADS + LOADS)

                def timely_batch(b):
                    act.wait_ge(s_added, b * 2 * EVERY + 2 * AHEAD + n * NG)
                    yield from batch(b, timely[n])
                if n == EDGE:
                    act.wait_ge(s_nodes, 32)
                with_batches(act, pair, timely_batch)
                if n == EDGE:
                    weight_column(FULL - 1, 0, PER_SLOT * LOADS)
                    weight_column(FULL, 1, PER_SLOT * LOADS)
                act.wait_ge(s_added, (n + 1) * NG)
                for _ in batch(NB - 1, timely[n]):
                    pass
                act.wait_ge(s_flag, 1)
                outside_any = act.value_load(flag[0:1, 0:1], min_val=0, max_val=P)
                with act.If(outside_any > 0):
                    act.wait_ge(r_added[n], NG * TILES)
                    act.wait_ge(timely[n].stored, stored_all(n))
                    with act.Fori(0, NB - 1) as b:
                        for _ in batch(b, again[n]):
                            pass
                    for _ in batch(NB - 1, again[n]):
                        pass
                    act.wait_ge(again[n].stored, stored_all(n))
            act.wait_ge(timely[BI].stored, stored_all(BI))

        @block.vector
        def _(dve):
            chain = Chain(dve, s_chain)
            slow_chain = Chain(dve, r_chain)
            steps_before = slow_steps_before = 0
            nc.vector.memset(nodes[0][:, TILES - 1, :], 0.0).then_inc(s_mem, 1)
            for s in (0, 1):
                nc.vector.memset(rows[s][:, :, D:D + 1], 1.0).then_inc(s_mem, 1)
            nc.vector.memset(top[:, :], 0.0).then_inc(s_spread, 1)
            nc.vector.memset(low[:, :], 0.0).then_inc(s_spread, 1)
            nc.vector.memset(ones[:, :], 1.0).then_inc(s_prep, 1)
            nc.vector.memset(limit[:, :], 0.0).then_inc(s_limit, 1)
            nc.vector.memset(ahead[:, :], 0.0).then_inc(s_limit, 1)
            dve.wait_ge(s_const, 11 * 16)
            dve.wait_ge(s_ident, 2)
            nc.vector.tensor_tensor(w0_own[:, :], w0_sb[:, 0, :], w0_sb[:, 1, :], ALU.subtract).then_inc(s_prep, 1)
            nc.vector.tensor_copy(w0_sums[:, :], ident[0:SR, 0:SR]).then_inc(s_prep, 1)
            dve.wait_ge(s_prep, 3)
            nc.vector.tensor_copy(w0_sums[0:D, 0:D], w0_sb[:, 1, :]).then_inc(s_prep, 1)
            dve.wait_ge(s_iota, 2)

            def turn_to_match(n, g, s, offsets, equal, matched, count):
                p, c = shape_of(g)
                nc.vector.tensor_tensor(match[s][0:p, 0:c, :],
                                        iota[0:p, :].unsqueeze(1).to_broadcast([p, c, P]),
                                        offsets[0:p, 0:c].unsqueeze(2).to_broadcast([p, c, P]),
                                        ALU.is_equal).then_inc(equal if WEIGHTED[n] else matched, 1)
                if WEIGHTED[n]:
                    dve.wait_ge(equal, count)
                    nc.vector.tensor_tensor(match[s][0:p, 0:c, :], match[s][0:p, 0:c, :],
                                            weight[s][0:p, 0:c].unsqueeze(2).to_broadcast([p, c, P]),
                                            ALU.mult).then_inc(matched, 1)

            for n in range(4):
                height = SR if n == EDGE else D
                if n:
                    dve.wait_ge(timely[n - 1].staged, NB * (1 if n - 1 == NORM else 2))
                nc.vector.memset(sums[0:height, :], 0.0).then_inc(s_cleared, 1)
                weighted_before = sum(WEIGHTED[:n]) * NG

                def build_match(g, s, loads):
                    p, c = shape_of(g)
                    at = g + n * NG
                    dve.wait_ge(s_loaded[s], loads)
                    nc.vector.tensor_scalar(offset[s][0:p, 0:c], dst_ix[s][0:p, 0:c], first[s][0:p, 0:1], None,
                                            ALU.subtract).then_inc(s_offset, 1)
                    dve.wait_ge(s_offset, at + 1)
                    if n == EDGE:
                        dve.wait_ge(s_spread, 2 * g + 2)
                        nc.vector.tensor_tensor(top[0:p, 0:c], top[0:p, 0:c], offset[s][0:p, 0:c],
                                                ALU.max).then_inc(s_spread, 1)
                        nc.vector.tensor_tensor(low[0:p, 0:c], low[0:p, 0:c], offset[s][0:p, 0:c],
                                                ALU.min).then_inc(s_spread, 1)
                    turn_to_match(n, g, s, offset[s], s_equal, s_match, g + weighted_before + 1)

                def add_part(g, s):
                    at = g + n * NG
                    node = dve.value_load(first[s][0:1, 0:1], min_val=0, max_val=V - 1)
                    if n == EDGE:
                        dve.wait_ge(s_limit, limits(g) + 2)
                        nc.vector.tensor_scalar(ahead[:, 0:1], first[s][:, 0:1], limit[:, 0:1], None,
                                                ALU.subtract).then_inc(s_limit, 1)
                        dve.wait_ge(s_limit, limits(g) + 3)
                        nc.vector.tensor_tensor(ahead[:, 1:2], ahead[:, 1:2], ahead[:, 0:1],
                                                ALU.min).then_inc(s_limit, 1)
                    dve.wait_ge(s_part, at + 1)
                    if not (isinstance(at, int) and at == 0):
                        dve.wait_ge(s_added, at)
                    nc.vector.tensor_tensor(sums[0:height, bass.ds(node, P)], sums[0:height, bass.ds(node, P)],
                                            part[s][0:height, :], ALU.add).then_inc(s_added, 1)

                def layer_norm(b, at, chain):
                    own = nodes[(n + 1) % 2][:, bass.ds(b * TB, TB), :]
                    chain.step(nc.vector.tensor_reduce(small[:, 4, 0:TB], work[:, :, :], AX.X, ALU.add))
                    chain.step(nc.vector.tensor_scalar(small[:, 4, 0:TB], small[:, 4, 0:TB], 1.0 / D, None, ALU.mult))
                    chain.step(nc.vector.tensor_tensor(work[:, :, :], work[:, :, :],
                                                       small[:, 4, 0:TB].unsqueeze(2).to_broadcast([P, TB, D]),
                                                       ALU.subtract))
                    chain.step(nc.vector.tensor_tensor(work2[:, :, :], work[:, :, :], work[:, :, :], ALU.mult))
                    chain.step(nc.vector.tensor_reduce(small[:, 5, 0:TB], work2[:, :, :], AX.X, ALU.add))
                    chain.step(nc.vector.tensor_scalar(small[:, 5, 0:TB], small[:, 5, 0:TB], 1.0 / D, EPS,
                                                       ALU.mult, ALU.add))
                    nc.vector.reciprocal(small[:, 6, 0:TB], small[:, 5, 0:TB]).then_inc(at.root_in, 1)
                    yield
                    dve.wait_ge(at.root, b * ROOTS[n] + ROOTS[n])
                    if not (isinstance(b, int) and b == 0):
                        dve.wait_ge(at.stored, b * 16)
                    rstd = small[:, 7, 0:TB].unsqueeze(2).to_broadcast([P, TB, D])
                    if n == BI:
                        last = nc.vector.tensor_tensor(result[:, :, :], work[:, :, :], rstd, ALU.mult)
                    else:
                        chain.step(nc.vector.tensor_tensor(own, work[:, :, :], rstd, ALU.mult))
                        if n == NORM:
                            last = nc.vector.tensor_tensor(result[:, :, :], work[:, :, :], rstd, ALU.mult)
                        else:
                            scale = gcn_scale if n == EDGE else norm_scale
                            last = nc.vector.tensor_tensor(
                                result[:, :, :], own,
                                scale[:, bass.ds(b * TB, TB)].unsqueeze(2).to_broadcast([P, TB, D]), ALU.mult)
                    last.then_inc(at.result, 1)
                    dve.wait_ge(at.result, b + 1)

                def spread_bias(k):
                    return bias[:, k, :].unsqueeze(1).to_broadcast([P, TB, D])

                def batch(b, at, chain):
                    own = nodes[n % 2][:, bass.ds(b * TB, TB), :]
                    if n == BI:
                        dve.wait_ge(at.turned, b + 1)
                        nc.vector.tensor_tensor(feats_b[:, :], feats_ps[:, 0:BATCH], sums_b[0:D, :],
                                                ALU.add).then_inc(at.feats, 1)
                        nc.vector.tensor_tensor(prod_b[:, :], feats_ps[:, 0:BATCH], sums_b[0:D, :],
                                                ALU.mult).then_inc(at.feats, 1)
                    yield
                    dve.wait_ge(at.prods, b + 1)
                    msg = first_ps[:, :, 0:D]
                    if n == EDGE:
                        count, degree = first_ps[:, :, D], first_ps[:, :, D + 1]
                        chain.step(nc.vector.tensor_scalar(small[:, 0, 0:TB], count, 1.0, None, ALU.max))
                        chain.step(nc.vector.tensor_scalar(small[:, 1, TB:2 * TB], degree, FILL, None, ALU.add))
                        chain.step(nc.vector.tensor_scalar(small[:, 0, TB:2 * TB], small[:, 1, TB:2 * TB], 1e-30, None,
                                                           ALU.max))
                        chain.step(nc.vector.tensor_scalar(small[:, 4, TB:2 * TB], small[:, 1, TB:2 * TB], 0.0, None,
                                                           ALU.is_gt))
                        nc.vector.reciprocal(small[:, 2, :], small[:, 0, :]).then_inc(at.root_in, 1)
                        chain.step(nc.vector.tensor_scalar(small[:, 4, 0:TB], count, 0.0, None, ALU.is_gt))
                        dve.wait_ge(at.root_in, b * 2 + 1)
                        chain.step(nc.vector.tensor_tensor(work[:, :, :], msg,
                                                           small[:, 2, 0:TB].unsqueeze(2).to_broadcast([P, TB, D]),
                                                           ALU.mult))
                        nc.vector.tensor_tensor(work2[:, :, :], work[:, :, :], second_ps[:, :, :],
                                                ALU.add).then_inc(at.taken, 1)
                        dve.wait_ge(at.taken, b + 1)
                        chain.step(nc.vector.tensor_tensor(work2[:, :, :], work2[:, :, :], spread_bias(0), ALU.add))
                        chain.step(nc.vector.tensor_tensor(work2[:, :, :], work2[:, :, :],
                                                           small[:, 4, 0:TB].unsqueeze(2).to_broadcast([P, TB, D]),
                                                           ALU.mult))
                        chain.step(nc.vector.tensor_tensor(work[:, :, :], work2[:, :, :], own, ALU.add))
                        yield
                        dve.wait_ge(at.root, b * 2 + 1)
                        chain.step(nc.vector.reciprocal(small[:, 5, :], small[:, 3, :]))
                        chain.step(nc.vector.tensor_tensor(small[:, 5, :], small[:, 5, :], small[:, 2, :], ALU.mult))
                        chain.step(nc.vector.tensor_tensor(small[:, 5, :], small[:, 5, :], small[:, 3, :], ALU.add))
                        chain.step(nc.vector.tensor_scalar(small[:, 5, :], small[:, 5, :], 0.5, None, ALU.mult))
                        chain.step(nc.vector.tensor_copy(norm_scale[:, bass.ds(b * TB, TB)], small[:, 5, 0:TB]))
                        chain.step(nc.vector.tensor_tensor(gcn_scale[:, bass.ds(b * TB, TB)], small[:, 5, TB:2 * TB],
                                                           small[:, 4, TB:2 * TB], ALU.mult))
                        chain.step(nc.vector.tensor_scalar(small[:, 5, 0:TB], gcn_scale[:, bass.ds(b * TB, TB)],
                                                           FILL, None, ALU.mult))
                        chain.step(nc.vector.tensor_tensor(gcn_loop[:, bass.ds(b * TB, TB)],
                                                           gcn_scale[:, bass.ds(b * TB, TB)], small[:, 5, 0:TB],
                                                           ALU.mult))
                    if n == GCN:
                        chain.step(nc.vector.tensor_tensor(
                            work[:, :, :], msg,
                            gcn_scale[:, bass.ds(b * TB, TB)].unsqueeze(2).to_broadcast([P, TB, D]), ALU.mult))
                        nc.vector.tensor_tensor(
                            work2[:, :, :], second_ps[:, :, :],
                            gcn_loop[:, bass.ds(b * TB, TB)].unsqueeze(2).to_broadcast([P, TB, D]),
                            ALU.mult).then_inc(at.taken, 1)
                        dve.wait_ge(at.taken, b + 1)
                        chain.step(nc.vector.tensor_tensor(work[:, :, :], work[:, :, :], work2[:, :, :], ALU.add))
                        nc.vector.tensor_tensor(work[:, :, :], work[:, :, :], spread_bias(1),
                                                ALU.add).then_inc(at.root_in, 1)
                        yield
                        dve.wait_ge(at.root, b * 2 + 1)
                        chain.step(nc.vector.tensor_tensor(work[:, :, :], work2[:, :, :], own, ALU.add))
                    if n == NORM:
                        nc.vector.tensor_tensor(
                            work[:, :, :], msg,
                            norm_scale[:, bass.ds(b * TB, TB)].unsqueeze(2).to_broadcast([P, TB, D]),
                            ALU.mult).then_inc(at.taken, 1)
                        dve.wait_ge(at.taken, b + 1)
                        yield
                        chain.step(nc.vector.tensor_tensor(work[:, :, :], work[:, :, :], spread_bias(2), ALU.add))
                        chain.step(nc.vector.tensor_tensor(work[:, :, :], work[:, :, :], own, ALU.add))
                    if n == BI:
                        chain.step(nc.vector.tensor_tensor(work[:, :, :], msg, spread_bias(3), ALU.add))
                        nc.vector.tensor_tensor(work2[:, :, :], second_ps[:, :, :], spread_bias(4),
                                                ALU.add).then_inc(at.taken, 1)
                        chain.step(nc.vector.scalar_tensor_tensor(work[:, :, :], work[:, :, :], SLOPE, work[:, :, :],
                                                                  ALU.mult, ALU.max))
                        yield
                        dve.wait_ge(at.taken, b + 1)
                        chain.step(nc.vector.scalar_tensor_tensor(work2[:, :, :], work2[:, :, :], SLOPE,
                                                                  work2[:, :, :], ALU.mult, ALU.max))
                        chain.step(nc.vector.tensor_tensor(work[:, :, :], work[:, :, :], work2[:, :, :], ALU.add))
                        chain.step(nc.vector.tensor_tensor(work[:, :, :], work[:, :, :], own, ALU.add))
                    yield from layer_norm(b, at, chain)

                before = n * PER_SLOT * LOADS
                each = {EDGE: 17 + 7, GCN: 3 + 7, NORM: 2 + 7, BI: 5 + 6}[n]
                turns_done = [0]

                def limits(g):
                    return 2 * g + turns_done[0]

                def pair(i):
                    build_match(2 * i + 1, 1, i * LOADS + before + LOADS)
                    add_part(2 * i, 0)
                    build_match(2 * i + 2, 0, i * LOADS + before + 2 * LOADS)
                    add_part(2 * i + 1, 1)

                def timely_batch(b):
                    if n == EDGE:
                        dve.wait_ge(s_limit, 2 * (b * 2 * EVERY + 2 * AHEAD) + b + 2)
                        nc.vector.tensor_scalar(limit[:, :], limit[:, :], float(BATCH), None,
                                                ALU.add).then_inc(s_limit, 1)
                        turns_done[0] = b + 1
                    chain.begin(b * each + steps_before)
                    yield from batch(b, timely[n], chain)
                    assert chain.k == each, (n, chain.k)

                build_match(0, 0, before + LOADS)
                dve.wait_ge(s_cleared, n + 1)
                if n == EDGE:
                    dve.wait_ge(s_nodes, 32)
                with_batches(dve, pair, timely_batch)
                steps_before += (NB - 1) * each
                build_match(FULL, 1, before + PER_SLOT * LOADS)
                add_part(FULL - 1, 0)
                add_part(FULL, 1)

                if n == EDGE:
                    chain.begin(steps_before)
                    dve.wait_ge(s_spread, 2 * NG + 2)
                    dve.wait_ge(s_limit, 2 * NG + 2 + NB - 1)
                    chain.step(nc.vector.tensor_reduce(spread[:, 0:1], top[:, :], AX.X, ALU.max))
                    chain.step(nc.vector.tensor_reduce(spread[:, 1:2], low[:, :], AX.X, ALU.min))
                    chain.step(nc.vector.tensor_scalar(spread[:, 2:3], spread[:, 0:1], float(P), None, ALU.is_ge))
                    chain.step(nc.vector.tensor_tensor(spread[:, 1:2], spread[:, 1:2], ahead[:, 1:2], ALU.min))
                    chain.step(nc.vector.tensor_scalar(spread[:, 3:4], spread[:, 1:2], 0.0, None, ALU.is_lt))
                    nc.vector.tensor_tensor(spread[:, 2:3], spread[:, 2:3], spread[:, 3:4],
                                            ALU.max).then_inc(s_prep, 1)
                    steps_before += chain.k
                    dve.wait_ge(s_out_ps, 1)
                    nc.vector.tensor_copy(flag[0:1, 0:1], second_ps[0:1, 0, 0:1]).then_inc(s_flag, 1)
                chain.begin(steps_before)
                for _ in batch(NB - 1, timely[n], chain):
                    pass
                steps_before += each
                dve.wait_ge(s_flag, 1)
                outside_any = dve.value_load(flag[0:1, 0:1], min_val=0, max_val=P)
                with dve.If(outside_any > 0):
                    def slow_group(g, done_groups):
                        p, c = shape_of(g)
                        per_window, head = SLOW[n]
                        base = done_groups * (head + TILES * per_window)
                        dve.wait_ge(r_loaded[n], done_groups * LOADS + LOADS)
                        steps = [
                            lambda: nc.vector.tensor_scalar(offset[0][0:p, 0:c], dst_ix[0][0:p, 0:c],
                                                            first[0][0:p, 0:1], None, ALU.subtract),
                            lambda: nc.vector.tensor_scalar(outside[0:p, 0:c, 0], offset[0][0:p, 0:c], 0.0, None,
                                                            ALU.is_ge),
                            lambda: nc.vector.scalar_tensor_tensor(outside[0:p, 0:c, 1], offset[0][0:p, 0:c],
                                                                   float(P), outside[0:p, 0:c, 0],
                                                                   ALU.is_lt, ALU.mult),
                            lambda: nc.vector.scalar_tensor_tensor(offset[1][0:p, 0:c], outside[0:p, 0:c, 1],
                                                                   float(2 * VP), dst_ix[0][0:p, 0:c],
                                                                   ALU.mult, ALU.add),
                        ]
                        if n == EDGE:
                            steps.append(lambda: nc.vector.tensor_copy(rows[0][0:p, 0:c, D + 1],
                                                                       weight[0][0:p, 0:c]))
                        for k, step in enumerate(steps):
                            step().then_inc(r_match[n], 1)
                            steps_done = held(dve, base + k + 1)
                            dve.wait_ge(s_flag, 1)
                            dve.wait_ge(r_match[n], steps_done)
                        with dve.Fori(0, TILES) as w:
                            now = w * per_window + base + head
                            nc.vector.tensor_tensor(match[0][0:p, 0:c, :],
                                                    iota[0:p, :].unsqueeze(1).to_broadcast([p, c, P]),
                                                    offset[1][0:p, 0:c].unsqueeze(2).to_broadcast([p, c, P]),
                                                    ALU.is_equal).then_inc(r_match[n], 1)
                            dve.wait_ge(r_match[n], now + 1)
                            if WEIGHTED[n]:
                                nc.vector.tensor_tensor(match[0][0:p, 0:c, :], match[0][0:p, 0:c, :],
                                                        weight[0][0:p, 0:c].unsqueeze(2).to_broadcast([p, c, P]),
                                                        ALU.mult).then_inc(r_match[n], 1)
                                dve.wait_ge(r_match[n], now + 2)
                            nc.vector.tensor_scalar(offset[1][0:p, 0:c], offset[1][0:p, 0:c], float(P), None,
                                                    ALU.subtract).then_inc(r_match[n], 1)
                            dve.wait_ge(r_part[n], w + done_groups * TILES + 1)
                            nc.vector.tensor_tensor(sums[0:height, bass.ds(w * P, P)],
                                                    sums[0:height, bass.ds(w * P, P)],
                                                    part[0][0:height, :], ALU.add).then_inc(r_added[n], 1)
                            dve.wait_ge(r_added[n], w + done_groups * TILES + 1)
                            dve.wait_ge(r_match[n], now + per_window)
                    with dve.Fori(0, FULL) as g:
                        slow_group(None, g)
                    slow_group(FULL, FULL)
                    with dve.Fori(0, NB - 1) as b:
                        slow_chain.begin(b * each + slow_steps_before)
                        for _ in batch(b, again[n], slow_chain):
                            pass
                    slow_chain.begin(slow_steps_before + (NB - 1) * each)
                    for _ in batch(NB - 1, again[n], slow_chain):
                        pass
                    slow_steps_before += NB * each

        @block.tensor
        def _(pe):
            def sum_by_node(n, g, s, done):
                p, c = shape_of(g)
                height = SR if n == EDGE else D
                for j in range(c):
                    last = nc.tensor.matmul(part[s][0:height, :], rows[s][0:p, j, 0:height], match[s][0:p, j, :],
                                            start=(j == 0), stop=(j == c - 1))
                last.then_inc(done, 1)

            for n in range(4):
                def sum_group(g, s, rows_in):
                    at = g + n * NG
                    pe.wait_ge(s_rows[n][s], rows_in)
                    pe.wait_ge(s_match, at + 1)
                    if n == EDGE:
                        pe.wait_ge(s_wcol, at + 1)
                    sum_by_node(n, g, s, s_part)
                ROWS = CHUNKS * 16

                def pair(i):
                    sum_group(2 * i, 0, i * ROWS + ROWS)
                    sum_group(2 * i + 1, 1, i * ROWS + ROWS)

                def batch(b, at):
                    height = SR if n == EDGE else D
                    before = not (isinstance(b, int) and b == 0)
                    feats = 2 if n == BI else 1
                    if n != NORM:
                        staged, read = held(pe, b * 2 + 2), held(pe, b * feats)
                        pe.wait_ge(s_ident, 2)
                        pe.wait_ge(at.staged, staged)
                        if before:
                            pe.wait_ge(at.feats, read)
                        for t in range(TB):
                            last = nc.tensor.transpose(feats_ps[:, t * P:(t + 1) * P], nodes_b[:, t, :], ident[:, :])
                        last.then_inc(at.turned, 1)
                    if n == NORM:
                        pe.wait_ge(at.staged, b + 1)
                    else:
                        pe.wait_ge(at.feats, b * feats + feats)
                    if before:
                        pe.wait_ge(at.taken, b)
                    first_w = (w0_sums[:, :], w1_sb[:, :], w2_sb[:, :], w_gc_sb[:, :])[n]
                    second_w = (w0_own[:, :], w1_sb[:, :], None, w_bi_sb[:, :])[n]
                    first_in = feats_b if n == BI else sums_b
                    second_in = prod_b if n == BI else feats_b
                    for t in range(TB):
                        last = nc.tensor.matmul(first_ps[:, t, 0:height], first_in[0:height, t * P:(t + 1) * P],
                                                first_w, start=True, stop=True)
                        if second_w is not None:
                            last = nc.tensor.matmul(second_ps[:, t, :], second_in[:, t * P:(t + 1) * P],
                                                    second_w, start=True, stop=True)
                    last.then_inc(at.prods, 1)
                    yield

                pe.wait_ge(s_prep, 4)
                with_batches(pe, pair, lambda b: batch(b, timely[n]))
                sum_group(FULL - 1, 0, PER_SLOT * ROWS)
                sum_group(FULL, 1, (PER_SLOT - 1) * ROWS + TAIL_C * 16)

                if n == EDGE:
                    pe.wait_ge(s_prep, 5)
                    nc.tensor.matmul(second_ps[0:1, 0, 0:1], spread[:, 2:3], ones[:, 0:1], start=True,
                                     stop=True).then_inc(s_out_ps, 1)
                pe.wait_ge(s_flag, 1)
                for _ in batch(NB - 1, timely[n]):
                    pass
                outside_any = pe.value_load(flag[0:1, 0:1], min_val=0, max_val=P)
                with pe.If(outside_any > 0):
                    per_window, head = SLOW[n]

                    def slow_group(g, done_groups, rows_in):
                        rows_held = [held(pe, v) for v in rows_in]
                        pe.wait_ge(s_flag, 1)
                        for j in (0, 1):
                            pe.wait_ge(r_rows[n][j], rows_held[j])
                        with pe.Fori(0, TILES) as w:
                            pe.wait_ge(r_match[n], w * per_window + done_groups * (head + TILES * per_window)
                                       + head + per_window)
                            sum_by_node(n, g, 0, r_part[n])
                    half = CHUNKS // 2 * 16
                    with pe.Fori(0, FULL) as g:
                        slow_group(None, g, [g * half + half] * 2)
                    slow_group(FULL, FULL, [FULL * half + (TAIL_C + 1) // 2 * 16, FULL * half + TAIL_C // 2 * 16])

                    with pe.Fori(0, NB - 1) as b:
                        for _ in batch(b, again[n]):
                            pass
                    for _ in batch(NB - 1, again[n]):
                        pass


_INS = ['x', 'src', 'dst', 'edge_weight', 'L0_gnn_W', 'L0_gnn_b', 'L1_gnn_W', 'L1_gnn_b', 'L2_gnn_weight',
        'L2_gnn_bias', 'L3_gnn_W_gc', 'L3_gnn_b_gc', 'L3_gnn_W_bi', 'L3_gnn_b_bi']


def kernel(**inputs):
    import numpy as _np
    import concourse.bacc as _bacc
    from concourse import mybir as _mybir
    from concourse.bass_utils import run_bass_kernel_spmd as _run

    nc = _bacc.Bacc("TRN2", target_bir_lowering=False, num_devices=1)
    arrays, args = {}, []
    for name in _INS:
        a = _np.ascontiguousarray(inputs[name])
        arrays[f"in_{name}_dram"] = a
        args.append(nc.dram_tensor(f"in_{name}_dram", a.shape, _mybir.dt.from_np(a.dtype), kind="ExternalInput").ap())
    out = nc.dram_tensor("out_0_dram", arrays["in_x_dram"].shape, _mybir.dt.float32, kind="ExternalOutput").ap()
    build(nc, *args, out)
    r = _run(nc, [arrays], core_ids=[0])
    return r.results[0]["out_0_dram"]
```
